# Optimizing a Trainium2 kernel written in Bass

```python
import numpy as np
import jax
import jax.numpy as jnp

def _softmax(x, axis=-1):
    return jax.nn.softmax(x, axis=axis)

def _gelu(x):
    return jax.nn.gelu(x, approximate=True)

def _silu(x):
    return jax.nn.silu(x)

def _sigmoid(x):
    return jax.nn.sigmoid(x)

def _layernorm(x, axis=-1, eps=1e-05):
    m = jnp.mean(x, axis=axis, keepdims=True)
    v = jnp.var(x, axis=axis, keepdims=True)
    return (x - m) / jnp.sqrt(v + eps)

def _scatter_add(tgt, idx, src, axis=0):
    return tgt.at[idx].add(src)

def _segment_sum(src, seg, n):
    return jax.ops.segment_sum(src, seg, n)
kernel_name = 'mk_gnn_resnorm_d1_gnn_r32_69c59c'

def setup_inputs(seed: int=0):
    np.random.seed(seed)
    _w = jnp.asarray

    def _rec_inputs():
        import jax
        import jax.numpy as jnp
        _gk = jax.random.key(seed)
        x = -0.0003713 + 1 * jax.random.normal(jax.random.fold_in(_gk, 1), (3125, 256), jnp.float32)
        _s = jax.random.randint(jax.random.fold_in(_gk, 2), (25000,), 0, 3125, jnp.int32)
        _d = jax.random.randint(jax.random.fold_in(_gk, 3), (25000,), 0, 3125, jnp.int32)
        _loop = jnp.arange(3125, dtype=jnp.int32)
        src = jnp.concatenate([_s, _d, _loop])
        dst = jnp.concatenate([_d, _s, _loop])
        _o = jnp.argsort(dst, stable=True)
        src = src[_o]
        dst = dst[_o]
        edge_attr_50 = 0.000154925 + 1.00009 * jax.random.normal(jax.random.fold_in(_gk, 11), (53125, 50), jnp.float32)
        edge_weight = jax.random.uniform(jax.random.fold_in(_gk, 13), (53125,), jnp.float32, 0.0, 9.99998)
        return (x, src, dst, edge_attr_50, edge_weight)
    x, src, dst, edge_attr_50, edge_weight = _rec_inputs()

    def _L0_gnn_setup():
        import jax, jax.numpy as jnp
        import numpy as np
        N, E, H, G = (50000, 25000, 256, 50)
        CUTOFF = 10.0
        PI = float(np.pi)
        LOG2 = float(np.log(2.0))

        def ssp(x):
            return jax.nn.softplus(x) - LOG2
        key = jax.random.key(seed)
        ks = jax.random.split(key, 16)

        def lin(kw, kb, fan_in, fan_out):
            s = float(np.sqrt(6.0 / (fan_in + fan_out)))
            W = jax.random.uniform(kw, (fan_in, fan_out), minval=-s, maxval=s, dtype=jnp.float32)
            b = jnp.zeros((fan_out,), jnp.float32)
            return (W, b)
        h = jax.random.normal(ks[0], (N, H), dtype=jnp.float32)
        edge_index = jax.random.randint(ks[1], (2, E), 0, N, dtype=jnp.int64)
        edge_weight = jax.random.uniform(ks[2], (E,), dtype=jnp.float32) * CUTOFF
        edge_attr = jax.random.normal(ks[3], (E, G), dtype=jnp.float32)
        aw_W, aw_b = lin(ks[4], ks[5], H, H)
        m1_W, m1_b = lin(ks[6], ks[7], G, H)
        m2_W, m2_b = lin(ks[8], ks[9], H, H)
        o1_W, o1_b = lin(ks[10], ks[11], H, H)
        o2_W, o2_b = lin(ks[12], ks[13], H, H)
        return {'h': h, 'edge_index': edge_index, 'edge_weight': edge_weight, 'edge_attr': edge_attr, 'aw_W': aw_W, 'aw_b': aw_b, 'm1_W': m1_W, 'm1_b': m1_b, 'm2_W': m2_W, 'm2_b': m2_b, 'o1_W': o1_W, 'o1_b': o1_b, 'o2_W': o2_W, 'o2_b': o2_b}
    _L0_gnn_all = _L0_gnn_setup()
    _L0_gnn_in = {k: v for k, v in _L0_gnn_all.items() if k in ('aw_W', 'aw_b', 'm1_W', 'm1_b', 'm2_W', 'm2_b', 'o1_W', 'o1_b', 'o2_W', 'o2_b')}
    del _L0_gnn_all
    return {'x': x, 'src': src, 'dst': dst, 'edge_attr_50': edge_attr_50, 'edge_weight': edge_weight, 'L0_gnn_aw_W': _L0_gnn_in['aw_W'], 'L0_gnn_aw_b': _L0_gnn_in['aw_b'], 'L0_gnn_m1_W': _L0_gnn_in['m1_W'], 'L0_gnn_m1_b': _L0_gnn_in['m1_b'], 'L0_gnn_m2_W': _L0_gnn_in['m2_W'], 'L0_gnn_m2_b': _L0_gnn_in['m2_b'], 'L0_gnn_o1_W': _L0_gnn_in['o1_W'], 'L0_gnn_o1_b': _L0_gnn_in['o1_b'], 'L0_gnn_o2_W': _L0_gnn_in['o2_W'], 'L0_gnn_o2_b': _L0_gnn_in['o2_b']}

def reference(x, src, dst, edge_attr_50, edge_weight, L0_gnn_aw_W, L0_gnn_aw_b, L0_gnn_m1_W, L0_gnn_m1_b, L0_gnn_m2_W, L0_gnn_m2_b, L0_gnn_o1_W, L0_gnn_o1_b, L0_gnn_o2_W, L0_gnn_o2_b):
    import jax
    import jax.numpy as jnp

    def _L0_gnn_ref(h, edge_index, edge_weight, edge_attr, aw_W, aw_b, m1_W, m1_b, m2_W, m2_b, o1_W, o1_b, o2_W, o2_b):
        import jax, jax.numpy as jnp
        import numpy as np
        N, E, H, G = (50000, 25000, 256, 50)
        CUTOFF = 10.0
        PI = float(np.pi)
        LOG2 = float(np.log(2.0))

        def ssp(x):
            return jax.nn.softplus(x) - LOG2
        n_nodes = h.shape[0]
        h1 = h @ aw_W + aw_b
        C = 0.5 * (jnp.cos(edge_weight * (PI / CUTOFF)) + 1.0)
        Wf = ssp(ssp(edge_attr @ m1_W + m1_b) @ m2_W + m2_b)
        Wf = Wf * C[:, None]
        src, dst = (edge_index[0], edge_index[1])
        msg = h1[src] * Wf
        agg = jax.ops.segment_sum(msg, dst, num_segments=n_nodes)
        out = ssp(agg @ o1_W + o1_b) @ o2_W + o2_b
        return out
    edge_index = jnp.stack([src, dst])
    x = _layernorm(x + _L0_gnn_ref(x, edge_index, edge_weight, edge_attr_50, L0_gnn_aw_W, L0_gnn_aw_b, L0_gnn_m1_W, L0_gnn_m1_b, L0_gnn_m2_W, L0_gnn_m2_b, L0_gnn_o1_W, L0_gnn_o1_b, L0_gnn_o2_W, L0_gnn_o2_b), axis=-1)
    return x

_drawn_inputs = setup_inputs


def setup_inputs(seed=0):
    import zlib

    import numpy as np

    out = dict(_drawn_inputs(seed))
    spreads = {'L0_gnn_aw_b': (0.0, 0.1),
     'L0_gnn_m1_b': (0.0, 0.1),
     'L0_gnn_m2_b': (0.0, 0.1),
     'L0_gnn_o1_b': (0.0, 0.1),
     'L0_gnn_o2_b': (0.0, 0.1)}
    factors = {}
    for name, (base, spread) in spreads.items():
        noise = np.random.default_rng([zlib.crc32(name.encode()), seed]).standard_normal(out[name].shape)
        drawn = base * np.exp(spread * noise) if base else spread * noise
        out[name] = jnp.asarray(drawn.astype(out[name].dtype))
    for name, factor in factors.items():
        out[name] = (out[name] * factor).astype(out[name].dtype)
    return out
```

```python
from contextlib import ExitStack
import math

import concourse.bass as bass
from concourse import mybir

F32 = mybir.dt.float32
BF16 = mybir.dt.bfloat16
I32 = mybir.dt.int32
F32R = mybir.dt.float32r
ALU = mybir.AluOpType
ACT = mybir.ActivationFunctionType
AX = mybir.AxisListType.X

P = 128
TILES = 4
GE = TILES * P
WIN = 64
UNROLL = 4
LN2 = math.log(2.0)
EXP_MAX = 2.0 ** 60
CUTOFF = 10.0
EPS = 1e-5
LN_EXP_TABLE = 6


def positive(count):
    return not isinstance(count, int) or count > 0


def gnn_resnorm_kernel(nc, x, xT, attrT, src, dst, dst_groups, edge_weight,
                       aw_W, aw_b, m1_W, m1_b, m2_W, m2_b, o1_W, o1_b, o2_W, o2_b, out):
    N, F = out.shape
    NP = x.shape[0]
    NTILES = NP // P
    AR = attrT.shape[0]
    G = m1_W.shape[0]
    KF = F // P
    NT = src.shape[1]
    NG = NT // TILES
    NWIN = NP // WIN
    UNITS = (NTILES + 1) // 2
    H1_BEFORE_M1 = UNITS - 5
    CHUNKS = (NTILES + TILES - 1) // TILES
    assert KF == 2 and NG % UNROLL == 0 and N + WIN <= NP + WIN and NWIN * WIN == NP

    with ExitStack() as ctx:
        def sb(name, shape, dt=F32):
            return ctx.enter_context(nc.sbuf_tensor(name, shape, dt))

        def sem(name):
            return ctx.enter_context(nc.semaphore(name))

        psum = ctx.enter_context(nc.psum_tensor("psum", [P, 8, 512], F32))
        u1 = [psum[:, 2 * b:2 * b + 2, :] for b in range(2)]
        u2 = [psum[:, 4 + 2 * b:6 + 2 * b, :] for b in range(2)]
        win_sum = [psum[:, 2 * b, 0:KF * WIN].rearrange("p (k n) -> p k n", k=KF) for b in range(2)]
        lo_bc, hi_bc = psum[:, 2, 0:NG], psum[:, 3, 0:NG]

        h1_table = nc.dram_tensor("h1_table", (NP, F), F32, kind="Internal").ap()

        aw_sb = sb("aw_sb", [P, KF, F])
        m1_sb = sb("m1_sb", [P, F])
        m1_part = sb("m1_part", [P, 2, F], F32R)
        m2_sb = sb("m2_sb", [P, KF, F])
        o1_sb = sb("o1_sb", [P, KF, F])
        o2_sb = sb("o2_sb", [P, KF, F])
        aw_bias = sb("aw_bias", [P, F])
        o2_bias = sb("o2_bias", [P, F])
        o1_bias = sb("o1_bias", [P, KF])
        o1_bias_ln2 = sb("o1_bias_ln2", [P, KF])
        m2_bias = sb("m2_bias", [P, F])
        m2_rest = sb("m2_rest", [P, 2, F])
        m2_part = sb("m2_part", [P, 3, F], BF16)
        m2_bias_rows = sb("m2_bias_rows", [P, 2, F], BF16)
        ones_bf = sb("ones_bf", [P, P], BF16)
        src_sb = sb("src_sb", [P, NT], I32)
        dst_sb = sb("dst_sb", [P, NT], I32)
        rel = sb("rel", [P, NT])
        cut = sb("cut", [P, NT])
        turns = sb("turns", [P, NT], I32)
        dst_g = sb("dst_g", [NG, GE], I32)
        ident = sb("ident", [P, P])
        iota_i = sb("iota_i", [P, WIN], I32)
        iota = sb("iota", [P, WIN])
        span_ends = sb("span_ends", [NG, 2])
        ends_wide = sb("ends_wide", [NG, 2, P])
        base = sb("base", [P, NG])
        span = sb("span", [P, NG])
        widest = sb("widest", [P, 1])
        base_i = sb("base_i", [P, NG], I32)
        widest_i = sb("widest_i", [P, 1], I32)
        rel_slow = sb("rel_slow", [P, TILES])
        att = sb("att", [P, 2, 2 * GE])
        att_part = sb("att_part", [P, 2, 2 * GE], F32R)
        e1 = sb("e1", [P, 2, KF * GE])
        a1 = sb("a1", [P, 2, KF * GE])
        e2 = sb("e2", [P, 2, TILES * F])
        msg = sb("msg", [P, 4, TILES * F])
        idx_now = sb("idx_now", [P, 4, TILES], I32)
        sel = sb("sel", [P, 2, TILES, WIN])
        agg = sb("agg", [P, KF, NP + WIN])
        xT_sb = sb("xT_sb", [P, KF, NP])
        h1_sb = sb("h1_sb", [P, NTILES, F])
        z = sb("z", [P, NTILES, F])
        stats = sb("stats", [P, NTILES, 6])
        mv = sb("mv", [P, NTILES, 2])
        var_eps = sb("var_eps", [P, NTILES])
        rstd0 = sb("rstd0", [P, NTILES])
        rstd = sb("rstd", [P, NTILES])
        newton = sb("newton", [P, NTILES])
        shift = sb("shift", [P, NTILES])
        half_pi = sb("half_pi", [P, 1])
        half_one = sb("half_one", [P, 1])

        dst_loaded = sem("dst_loaded")
        edge_loaded = sem("edge_loaded")
        bias_loaded = sem("bias_loaded")
        m1_loaded = sem("m1_loaded")
        m2_loaded = sem("m2_loaded")
        aw_loaded = sem("aw_loaded")
        o_loaded = sem("o_loaded")
        XT_CUTS = [0, 768, 1536, 2304, NP]
        xT_loaded = [sem(f"xT_loaded{i}") for i in range(4)]
        x_loaded = sem("x_loaded")
        att_loaded = [sem(f"att_loaded{i}") for i in range(2)]
        consts_ready = sem("consts_ready")
        zeros_ready = sem("zeros_ready")
        setup_step = sem("setup_step")
        ends_ready = sem("ends_ready")
        ends_spread = sem("ends_spread")
        windows_ready = sem("windows_ready")
        m1_ready = sem("m1_ready")
        m2_bias_ready = sem("m2_bias_ready")
        turns_ready = sem("turns_ready")
        sin_done = sem("sin_done")
        cut_ready = sem("cut_ready")
        h1_done = sem("h1_done")
        h1_ready = sem("h1_ready")
        h1_stored = sem("h1_stored")
        xb_ready = sem("xb_ready")
        att_rounded = sem("att_rounded")
        att_ready = sem("att_ready")
        m1_done = sem("m1_done")
        exp1_done = sem("exp1_done")
        clamp1_done = sem("clamp1_done")
        ln1_done = sem("ln1_done")
        a1_ready = sem("a1_ready")
        m2_done = sem("m2_done")
        exp2_done = sem("exp2_done")
        clamp2_done = sem("clamp2_done")
        ln2_done = sem("ln2_done")
        wf_ready = sem("wf_ready")
        idx_ready = sem("idx_ready")
        gathered = [sem(f"gathered{i}") for i in range(4)]
        msg_ready = sem("msg_ready")
        sel_ready = sem("sel_ready")
        win_done = sem("win_done")
        agg_added = sem("agg_added")
        slow_rel = sem("slow_rel")
        slow_sel = sem("slow_sel")
        slow_win = sem("slow_win")
        slow_added = sem("slow_added")
        o1_done = sem("o1_done")
        oexp_done = sem("oexp_done")
        oclamp_done = sem("oclamp_done")
        oln_done = sem("oln_done")
        t_ready = sem("t_ready")
        o2_done = sem("o2_done")
        out_step = sem("out_step")
        z_ready = sem("z_ready")
        var_ready = sem("var_ready")
        lnv_done = sem("lnv_done")
        rstd0_ready = sem("rstd0_ready")
        scale_ready = sem("scale_ready")
        y_ready = sem("y_ready")
        stored = sem("stored")

        block = ctx.enter_context(nc.Block())

        def chunk_tiles(c):
            return min(TILES, NTILES - TILES * c)

        @block.sync
        def _(sp):
            sp.dma_start(dst_g[:, :], dst_groups).then_inc(dst_loaded, 16)
            sp.dma_start(aw_sb[:, :, :], aw_W.rearrange("(k p) f -> p k f", p=P)).then_inc(aw_loaded, 16)
            xT_v = xT.rearrange("(k p) n -> p k n", p=P)
            for i in range(4):
                a, b = XT_CUTS[i], XT_CUTS[i + 1]
                sp.dma_start(xT_sb[:, :, a:b], xT_v[:, :, a:b]).then_inc(xT_loaded[i], 16)
                if i == 0:
                    sp.dma_start(dst_sb[:, :], dst).then_inc(edge_loaded, 16)
                    sp.dma_start(cut[:, :], edge_weight).then_inc(edge_loaded, 16)
                    sp.dma_start(src_sb[:, :], src).then_inc(edge_loaded, 16)
                    sp.dma_start(aw_bias[:, :], aw_b.partition_broadcast(P)).then_inc(bias_loaded, 16)
                    sp.dma_start(m2_bias[:, :], m2_b.partition_broadcast(P)).then_inc(bias_loaded, 16)
                    sp.dma_start(o2_bias[:, :], o2_b.partition_broadcast(P)).then_inc(bias_loaded, 16)
                    sp.dma_start(o1_bias[:, :], o1_b).then_inc(bias_loaded, 16)
                if i == 1:
                    sp.wait_ge(zeros_ready, 1)
                    for r in (0, AR):
                        sp.dma_start(m1_sb[r:r + G, :], m1_W).then_inc(m1_loaded, 16)
                        sp.dma_start(m1_sb[r + G:r + G + 1, :], m1_b.rearrange("(a f) -> a f", a=1))\
                          .then_inc(m1_loaded, 16)
            for c in range(2):
                for r in range(2):
                    sp.dma_start(att[r * AR:(r + 1) * AR, c, :], attrT[:, c * 2 * GE:(c + 1) * 2 * GE])\
                      .then_inc(att_loaded[c], 16)
            sp.dma_start(m2_sb[:, :, :], m2_W.rearrange("(k p) f -> p k f", p=P)).then_inc(m2_loaded, 16)
            for u in range(UNITS):
                n = min(2, NTILES - 2 * u)
                sp.wait_ge(h1_ready, u + 1)
                sp.dma_start(h1_table[u * 2 * P:(u * 2 + n) * P, :].rearrange("(t p) f -> p t f", p=P),
                             h1_sb[:, 2 * u:2 * u + n, :]).then_inc(h1_stored, 16)
            def attributes(q, k):
                sp.wait_ge(att_ready, q * 2 + (k - 1))
                for r in range(2):
                    sp.dma_start(att[r * AR:(r + 1) * AR, k, :], attrT[:, bass.ds((q * 2 + k) * 2 * GE, 2 * GE)])\
                      .then_inc(att_loaded[k], 16)

            for q in range(1, 4):
                for k in range(2):
                    attributes(q, k)
            sp.dma_start(z[:, :, :], x.rearrange("(t p) f -> p t f", p=P)).then_inc(x_loaded, 16)
            sp.dma_start(o1_sb[:, :, :], o1_W.rearrange("(k p) f -> p k f", p=P)).then_inc(o_loaded, 16)
            sp.dma_start(o2_sb[:, :, :], o2_W.rearrange("(k p) f -> p k f", p=P)).then_inc(o_loaded, 16)
            with sp.Fori(4, NG // UNROLL) as q:
                for k in range(2):
                    attributes(q, k)
            for c in range(CHUNKS):
                sp.wait_ge(y_ready, c + 1)
                full = min(chunk_tiles(c), N // P - TILES * c)
                if full > 0:
                    sp.dma_start(out[c * GE:c * GE + full * P, :].rearrange("(t p) f -> p t f", p=P),
                                 z[:, TILES * c:TILES * c + full, :]).then_inc(stored, 16)
                if full < chunk_tiles(c):
                    sp.dma_start(out[N // P * P:N, :], z[0:N % P, N // P, :]).then_inc(stored, 16)
            stores = sum((min(chunk_tiles(c), N // P - TILES * c) > 0)
                         + (min(chunk_tiles(c), N // P - TILES * c) < chunk_tiles(c)) for c in range(CHUNKS))
            sp.wait_ge(stored, 16 * stores)

        @block.gpsimd
        def _(pool):
            pool.memset(ident[:, :], 0.0).then_inc(consts_ready, 1)
            pool.wait_ge(consts_ready, 1)
            pool.affine_select(out=ident[:, :], in_=ident[:, :], compare_op=ALU.not_equal, fill=1.0, base=0,
                               pattern=[[-1, P]], channel_multiplier=1).then_inc(consts_ready, 1)
            pool.iota(iota_i[:, :], [[1, WIN]], base=0, channel_multiplier=0).then_inc(consts_ready, 1)
            nc.gpsimd.memset(agg[:, :, :], 0.0).then_inc(slow_added, 1)
            pool.wait_ge(edge_loaded, 48)

            def copy_indices(g, k):
                pool.tensor_copy(idx_now[:, k, :], src_sb[:, bass.ds(g * TILES, TILES)]).then_inc(idx_ready, 1)

            def gather(g, k, q, last=False):
                if positive(g - 3):
                    pool.wait_ge(win_done, g - 3)
                if not last and positive(q + k // 3):
                    pool.wait_ge(gathered[(k + 1) % 4], q * (16 * TILES) + k // 3 * 16 * TILES)
                pool.wait_ge(idx_ready, g + 1)
                if not last:
                    copy_indices(g + 1, (k + 1) % 4)
                for j in range(TILES):
                    pool.indirect_dma_start(msg[:, k, j * F:(j + 1) * F], None, h1_table,
                                            bass.IndirectOffsetOnAxis(idx_now[:, k, j:j + 1], 0))\
                        .then_inc(gathered[k], 16)

            def low_parts(c, slot):
                low = slice(0, AR)
                pool.wait_ge(att_rounded, c + 1)
                pool.tensor_tensor(att_part[low, slot, :], att[low, slot, :], att_part[low, slot, :].bitcast(F32),
                                   ALU.subtract).then_inc(att_ready, 1)

            low_parts(0, 0)
            low_parts(1, 1)
            copy_indices(0, 0)
            pool.wait_ge(h1_stored, 16 * UNITS)
            for k in range(4):
                gather(k, k, 0)
                if k == 1:
                    low_parts(2, 0)
            with pool.Fori(1, NG // UNROLL - 1) as q:
                for k in range(4):
                    gather(q * UNROLL + k, k, q)
                    if k % 2 == 0:
                        low_parts(q * 2 + 1 + k // 2, (k // 2 + 1) % 2)
            for k in range(4):
                gather(NG - UNROLL + k, k, NG // UNROLL - 1, last=(k == 3))
                if k == 0:
                    low_parts(NG // 2 - 1, 1)
            pool.wait_ge(x_loaded, 16)
            pool.wait_ge(bias_loaded, 64)
            for t in range(NTILES):
                last = pool.tensor_tensor(z[:, t, :], z[:, t, :], o2_bias[:, :], ALU.add)
            last.then_inc(xb_ready, 1)

        @block.scalar
        def _(act):
            act.wait_ge(turns_ready, 1)
            nc.scalar.activation(cut[:, :], cut[:, :], ACT.Abs).then_inc(sin_done, 1)
            act.wait_ge(sin_done, 1)
            nc.scalar.activation(cut[:, :], cut[:, :], ACT.Sin, bias=half_pi[:, 0:1],
                                 scale=-math.pi / (2 * CUTOFF)).then_inc(sin_done, 1)
            act.add_instruction(mybir.InstLoadActFuncSet(name=nc.get_next_instruction_name(),
                                                         act_func_set_id=LN_EXP_TABLE, ins=[], outs=[]))

            def round_attributes(c, slot, rounds):
                act.wait_ge(att_loaded[slot], 32 * rounds + 32)
                if positive(c - 1):
                    act.wait_ge(m1_done, c * 2 - 2)
                nc.scalar.activation(att_part[:, slot, :], att[:, slot, :], ACT.Copy).then_inc(att_rounded, 1)

            def exp1(g, k):
                b = k % 2
                act.wait_ge(m1_done, g + 1)
                if positive(g - 1):
                    act.wait_ge(a1_ready, g - 1)
                nc.scalar.activation(e1[:, b, :], u1[b], ACT.Exp).then_inc(exp1_done, 1)

            def ln1(g, k):
                b = k % 2
                act.wait_ge(clamp1_done, g + 1)
                nc.scalar.activation(e1[:, b, :], e1[:, b, :], ACT.Ln, bias=half_one[:, 0:1], scale=0.5)\
                  .then_inc(ln1_done, 1)

            def exp2(g, k):
                b = k % 2
                act.wait_ge(m2_done, g + 1)
                if positive(g - 1):
                    act.wait_ge(msg_ready, g - 1)
                nc.scalar.activation(e2[:, b, :], u2[b], ACT.Exp).then_inc(exp2_done, 1)

            def ln2(g, k):
                b = k % 2
                act.wait_ge(clamp2_done, g + 1)
                nc.scalar.activation(e2[:, b, :], e2[:, b, :], ACT.Ln, bias=half_one[:, 0:1], scale=0.5)\
                  .then_inc(ln2_done, 1)

            def step(s, k, q):
                edge = isinstance(s, int)
                if not edge or 0 <= s - 1 < NG:
                    exp2(s - 1, k - 1)
                if not edge or s + 1 < NG:
                    exp1(s + 1, k + 1)
                if not edge or 0 <= s - 1 < NG:
                    ln2(s - 1, k - 1)
                if not edge or s + 1 < NG:
                    ln1(s + 1, k + 1)
                if k % 2 == 0 and (not edge or s + 4 < NG):
                    round_attributes(q * 2 + 2 + k // 2, k // 2, q + 1)

            for c in range(2):
                round_attributes(c, c, 0)
            exp1(0, 0)
            ln1(0, 0)
            for s in range(UNROLL):
                step(s, s, 0)
            with act.Fori(1, NG // UNROLL - 1) as q:
                for k in range(UNROLL):
                    step(q * UNROLL + k, k, q)
            for s in range(NG - UNROLL, NG + 2):
                step(s, s % UNROLL, s // UNROLL)

            def o_exp(c):
                n = chunk_tiles(c) * P
                act.wait_ge(o1_done, c + 1)
                if c >= 2:
                    act.wait_ge(t_ready, c - 1)
                for h in range(KF):
                    last = nc.scalar.activation(e1[:, c % 2, h * GE:h * GE + n], u1[c % 2][:, h, 0:n], ACT.Exp,
                                                bias=o1_bias[:, h:h + 1])
                    if h == KF - 1:
                        last.then_inc(oexp_done, 1)

            def o_ln(c):
                n = chunk_tiles(c) * P
                act.wait_ge(oclamp_done, c + 1)
                ev = e1[:, c % 2, :].rearrange("p (h n) -> p h n", h=KF)[:, :, 0:n]
                nc.scalar.activation(ev, ev, ACT.Ln, bias=half_one[:, 0:1], scale=0.5).then_inc(oln_done, 1)

            def o_rstd(c):
                ts = slice(TILES * c, TILES * c + chunk_tiles(c))
                act.wait_ge(var_ready, c + 1)
                nc.scalar.activation(rstd0[:, ts], var_eps[:, ts], ACT.Ln).then_inc(lnv_done, 1)
                act.wait_ge(lnv_done, c + 1)
                nc.scalar.activation(rstd0[:, ts], rstd0[:, ts], ACT.Exp, scale=-0.5).then_inc(rstd0_ready, 1)

            def o_norm(c):
                act.wait_ge(scale_ready, c + 1)
                for t in range(TILES * c, TILES * c + chunk_tiles(c)):
                    last = nc.scalar.activation(z[:, t, :], z[:, t, :], ACT.Identity, bias=shift[:, t:t + 1],
                                                scale=rstd[:, t:t + 1])
                    if t == TILES * c + chunk_tiles(c) - 1:
                        last.then_inc(y_ready, 1)

            act.wait_ge(bias_loaded, 64)
            for c in range(CHUNKS + 2):
                if c < CHUNKS:
                    o_exp(c)
                if c >= 2:
                    o_rstd(c - 2)
                if c < CHUNKS:
                    o_ln(c)
                if c >= 2:
                    o_norm(c - 2)

        @block.tensor
        def _(pe):
            pe.wait_ge(consts_ready, 2)
            pe.wait_ge(ends_ready, 1)
            for e, spread in enumerate((lo_bc, hi_bc)):
                last = nc.tensor.matmul(spread, ends_wide[:, e, :], ident[0:NG, 0:NG], start=True, stop=True)
            last.then_inc(ends_spread, 1)

            def h1(u):
                n = min(2, NTILES - 2 * u)
                if u % 3 == 0 and u // 3 < 4:
                    pe.wait_ge(xT_loaded[u // 3], 16)
                if u >= 4:
                    pe.wait_ge(h1_ready, u - 3)
                bank = psum[:, 4 + u % 4, :]
                for j in range(n):
                    t = 2 * u + j
                    for kf in range(KF):
                        last = nc.tensor.matmul(bank[:, j * F:(j + 1) * F], xT_sb[:, kf, t * P:(t + 1) * P],
                                                aw_sb[:, kf, :], start=(kf == 0), stop=(kf == KF - 1))
                last.then_inc(h1_done, 1)

            def m1(g, k, c):
                b = k % 2
                pe.wait_ge(att_ready, c * 2 + k // 2 + 1)
                if positive(g - 3):
                    pe.wait_ge(agg_added, g - 3)
                for h in range(KF):
                    for part in range(2):
                        last = nc.tensor.matmul(u1[b][:, h, :], m1_part[:, part, h * P:(h + 1) * P],
                                                att_part[:, k // 2, k % 2 * GE:(k % 2 + 1) * GE],
                                                start=(part == 0), stop=(part == 1))
                last.then_inc(m1_done, 1)

            def m2(g, k):
                b = k % 2
                pe.wait_ge(a1_ready, g + 1)
                if positive(g - 1):
                    pe.wait_ge(wf_ready, g - 1)
                for h in range(2):
                    nc.tensor.matmul(u2[b][:, h, :], ones_bf[:, :], m2_bias_rows[:, :, :].rearrange("p a f -> p (a f)"),
                                     start=True, stop=False, skip_group_check=True)
                    for j in range(2):
                        for kf in range(KF):
                            e0 = kf * GE + (2 * h + j) * P
                            last = nc.tensor.matmul(u2[b][:, h, j * F:(j + 1) * F], a1[:, b, e0:e0 + P],
                                                    m2_sb[:, kf, :], start=False, stop=(kf == KF - 1),
                                                    skip_group_check=True)
                last.then_inc(m2_done, 1)

            def window(k, signal):
                for h in range(KF):
                    for j in range(TILES):
                        last = nc.tensor.matmul(win_sum[k % 2][:, h, :], msg[:, k, j * F + h * P:j * F + (h + 1) * P],
                                                sel[:, k % 2, j, :], start=(j == 0), stop=(j == TILES - 1))
                last.then_inc(signal, 1)

            def scatter(g, k, fits, last_group):
                def enter():
                    pe.wait_ge(msg_ready, g + 1)
                    if not last_group:
                        pe.wait_ge(a1_ready, g + 3)

                if not fits:
                    with pe.Fori(0, NWIN - 1) as w:
                        enter()
                        n = g * (NWIN - 1) + w
                        pe.wait_ge(slow_sel, n + 1)
                        pe.wait_ge(slow_added, n + 1)
                        window(k, slow_win)
                    pe.wait_ge(slow_added, (g + 1) * (NWIN - 1) + 1)
                enter()
                pe.wait_ge(sel_ready, g + 1)
                window(k, win_done)

            def step(s, k, fits, q):
                edge = isinstance(s, int)
                if not edge or 0 <= s - 2 < NG:
                    scatter(s - 2, (k - 2) % UNROLL, fits, edge and s >= NG)
                if not edge or s < NG:
                    m2(s, k)
                if not edge or s + 2 < NG:
                    m1(s + 2, (k + 2) % UNROLL, q + (k + 2) // UNROLL)

            pe.wait_ge(aw_loaded, 16)
            for u in range(H1_BEFORE_M1):
                h1(u)
            pe.wait_ge(m1_ready, 1)
            pe.wait_ge(windows_ready, 1)
            m1(0, 0, 0)
            m1(1, 1, 0)
            for u in range(H1_BEFORE_M1, UNITS):
                h1(u)
            pe.wait_ge(m2_loaded, 16)
            pe.wait_ge(m2_bias_ready, 1)
            pe.wait_ge(h1_ready, UNITS)
            widest_span = pe.value_load(widest_i[0:1, 0:1], min_val=0, max_val=NP)

            def edges(fits):
                for s in range(UNROLL):
                    step(s, s, fits, 0)
                with pe.Fori(1, NG // UNROLL - 1) as q:
                    for k in range(UNROLL):
                        step(q * UNROLL + k, k, fits, q)
                for s in range(NG - UNROLL, NG + 2):
                    step(s, s % UNROLL, fits, s // UNROLL)

            with pe.If(widest_span < WIN):
                edges(True)
            with pe.Else():
                edges(False)

            def o1(c):
                n = chunk_tiles(c) * P
                if c >= 2:
                    pe.wait_ge(t_ready, c - 1)
                for h in range(KF):
                    for kf in range(KF):
                        last = nc.tensor.matmul(u1[c % 2][:, h, 0:n], o1_sb[:, kf, h * P:(h + 1) * P],
                                                agg[:, kf, c * GE:c * GE + n], start=(kf == 0), stop=(kf == KF - 1))
                last.then_inc(o1_done, 1)

            def o2(c):
                pe.wait_ge(t_ready, c + 1)
                if c >= 2:
                    pe.wait_ge(z_ready, c - 1)
                for j in range(chunk_tiles(c)):
                    for kf in range(KF):
                        e0 = kf * GE + j * P
                        last = nc.tensor.matmul(u2[c % 2][:, j // 2, j % 2 * F:(j % 2 + 1) * F], a1[:, c % 2, e0:e0 + P],
                                                o2_sb[:, kf, :], start=(kf == 0), stop=(kf == KF - 1))
                last.then_inc(o2_done, 1)

            pe.wait_ge(o_loaded, 32)
            pe.wait_ge(agg_added, NG)
            o1(0)
            for c in range(CHUNKS):
                if c + 1 < CHUNKS:
                    o1(c + 1)
                o2(c)

        @block.vector
        def _(dve):
            done = [0]

            def link(ins):
                done[0] += 1
                ins.then_inc(setup_step, 1)
                dve.wait_ge(setup_step, done[0])

            nc.vector.memset(m1_sb[:, :], 0.0).then_inc(zeros_ready, 1)
            nc.vector.memset(half_pi[:, :], math.pi / 2)
            nc.vector.memset(half_one[:, :], 0.5)
            nc.vector.memset(ones_bf[:, :], 1.0)
            link(nc.vector.memset(ends_wide[:, :, :], 1.0))

            dve.wait_ge(dst_loaded, 16)
            nc.vector.tensor_reduce(span_ends[:, 0:1], dst_g[:, :], AX, ALU.min)
            link(nc.vector.tensor_reduce(span_ends[:, 1:2], dst_g[:, :], AX, ALU.max))
            for e in range(2):
                last = nc.vector.tensor_scalar(ends_wide[:, e, :], ends_wide[:, e, :], span_ends[:, e:e + 1], None, ALU.mult)
            last.then_inc(ends_ready, 1)
            dve.wait_ge(consts_ready, 3)
            nc.vector.tensor_copy(iota[:, :], iota_i[:, :])
            dve.wait_ge(edge_loaded, 48)
            link(nc.vector.tensor_scalar(turns[:, :], cut[:, :], 1.0 / (2 * CUTOFF), None, ALU.mult))
            nc.vector.scalar_tensor_tensor(out=cut[:, :], in0=turns[:, :], scalar=-2 * CUTOFF, in1=cut[:, :],
                                           op0=ALU.mult, op1=ALU.add).then_inc(turns_ready, 1)
            dve.wait_ge(ends_spread, 1)
            link(nc.vector.tensor_copy(base[:, :], lo_bc))
            link(nc.vector.tensor_tensor(span[:, :], hi_bc, base[:, :], ALU.subtract))
            link(nc.vector.tensor_reduce(widest[:, :], span[:, :], AX, ALU.max))
            nc.vector.tensor_copy(base_i[:, :], base[:, :])
            link(nc.vector.tensor_copy(widest_i[:, :], widest[:, :]))
            rel_v = rel[:, :].rearrange("p (g j) -> p g j", j=TILES)
            dst_v = dst_sb[:, :].rearrange("p (g j) -> p g j", j=TILES)
            for j in range(TILES):
                last = nc.vector.tensor_tensor(rel_v[:, :, j], dst_v[:, :, j], base[:, :], ALU.subtract)
            last.then_inc(windows_ready, 1)

            def m1_parts():
                dve.wait_ge(m1_loaded, 64)
                link(nc.vector.tensor_copy(m1_part[:, 0, :], m1_sb[:, :]))
                nc.vector.tensor_tensor(m1_part[:, 1, :], m1_sb[:, :], m1_part[:, 0, :].bitcast(F32), ALU.subtract)\
                  .then_inc(m1_ready, 1)

            def m2_bias_parts():
                link(nc.vector.tensor_copy(m2_part[:, 0, :], m2_bias[:, :]))
                link(nc.vector.tensor_tensor(m2_rest[:, 0, :], m2_bias[:, :], m2_part[:, 0, :], ALU.subtract))
                link(nc.vector.tensor_copy(m2_part[:, 1, :], m2_rest[:, 0, :]))

            def m2_bias_last_part():
                link(nc.vector.tensor_tensor(m2_rest[:, 1, :], m2_rest[:, 0, :], m2_part[:, 1, :], ALU.subtract))
                nc.vector.memset(m2_bias_rows[:, :, :], 0.0)
                link(nc.vector.tensor_copy(m2_part[:, 2, :], m2_rest[:, 1, :]))

            def m2_bias_to_rows():
                for i in range(3):
                    for twice in range(2):
                        last = nc.vector.tensor_copy(m2_bias_rows[32 * i:32 * i + 1, twice, :],
                                                     m2_part[32 * i:32 * i + 1, i, :])
                last.then_inc(m2_bias_ready, 1)

            def square_cosine():
                dve.wait_ge(sin_done, 2)
                nc.vector.tensor_tensor(cut[:, :], cut[:, :], cut[:, :], ALU.mult).then_inc(cut_ready, 1)
                nc.vector.tensor_scalar(o1_bias_ln2[:, :], o1_bias[:, :], -LN2, None, ALU.add)

            def clamp1(g, k):
                b = k % 2
                dve.wait_ge(exp1_done, g + 1)
                nc.vector.tensor_scalar(e1[:, b, :], e1[:, b, :], EXP_MAX, None, ALU.min).then_inc(clamp1_done, 1)

            def act1(g, k):
                b = k % 2
                dve.wait_ge(ln1_done, g + 1)
                if positive(g - 1):
                    dve.wait_ge(m2_done, g - 1)
                nc.vector.scalar_tensor_tensor(out=a1[:, b, :].rearrange("p (h e) -> p h e", h=KF), in0=u1[b],
                                               scalar=-LN2, in1=e1[:, b, :].rearrange("p (h e) -> p h e", h=KF),
                                               op0=ALU.add, op1=ALU.max).then_inc(a1_ready, 1)

            between = {1: m1_parts, 3: m2_bias_parts, 4: m2_bias_last_part, 5: m2_bias_to_rows, 6: square_cosine,
                       H1_BEFORE_M1 + 1: lambda: clamp1(0, 0), H1_BEFORE_M1 + 2: lambda: act1(0, 0)}
            dve.wait_ge(bias_loaded, 64)
            for u in range(UNITS):
                n = min(2, NTILES - 2 * u)
                dve.wait_ge(h1_done, u + 1)
                nc.vector.tensor_tensor(h1_sb[:, 2 * u:2 * u + n, :],
                                        psum[:, 4 + u % 4, 0:n * F].rearrange("p (t f) -> p t f", t=n),
                                        aw_bias[:, :].unsqueeze(1).to_broadcast([P, n, F]), ALU.add).then_inc(h1_ready, 1)
                if u in between:
                    between[u]()

            def clamp2(g, k):
                b = k % 2
                dve.wait_ge(exp2_done, g + 1)
                nc.vector.tensor_scalar(e2[:, b, :], e2[:, b, :], EXP_MAX, None, ALU.min).then_inc(clamp2_done, 1)

            def filt(g, k):
                b = k % 2
                dve.wait_ge(ln2_done, g + 1)
                ev = e2[:, b, :].rearrange("p (h e) -> p h e", h=2)
                nc.vector.scalar_tensor_tensor(out=ev, in0=u2[b], scalar=-LN2, in1=ev,
                                               op0=ALU.add, op1=ALU.max).then_inc(wf_ready, 1)

            def message(g, k, rounds):
                dve.wait_ge(gathered[k], rounds * (16 * TILES) + 16 * TILES)
                dve.wait_ge(wf_ready, g + 1)
                nc.vector.tensor_tensor(msg[:, k, :], e2[:, k % 2, :], msg[:, k, :], ALU.mult).then_inc(msg_ready, 1)

            def select(g, k, rels, signal):
                for j in range(TILES):
                    last = nc.vector.tensor_scalar(sel[:, k % 2, j, :], iota[:, :], rels[j],
                                                   cut[:, bass.ds(g * TILES + j, 1)], ALU.is_equal, ALU.mult)
                last.then_inc(signal, 1)

            def add_window(k, start, signal):
                nc.vector.tensor_tensor(agg[:, :, bass.ds(start, WIN)], agg[:, :, bass.ds(start, WIN)],
                                        win_sum[k % 2], ALU.add).then_inc(signal, 1)

            def select_own(g, k):
                if positive(g - 1):
                    dve.wait_ge(win_done, g - 1)
                select(g, k, [rel[:, bass.ds(g * TILES + j, 1)] for j in range(TILES)], sel_ready)

            def add_own(g, k, start):
                dve.wait_ge(win_done, g + 1)
                if positive(g):
                    dve.wait_ge(agg_added, g)
                add_window(k, start, agg_added)

            def add_all(g, k):
                if positive(g):
                    dve.wait_ge(sel_ready, g)
                nc.vector.tensor_copy(rel_slow[:, :], dst_sb[:, bass.ds(g * TILES, TILES)]).then_inc(slow_rel, 1)
                with dve.Fori(0, NWIN - 1) as w:
                    n = g * (NWIN - 1) + w
                    dve.wait_ge(slow_rel, g * NWIN + w + 1)
                    select(g, k, [rel_slow[:, j:j + 1] for j in range(TILES)], slow_sel)
                    dve.wait_ge(slow_sel, n + 1)
                    nc.vector.tensor_scalar(rel_slow[:, :], rel_slow[:, :], -float(WIN), None, ALU.add)\
                      .then_inc(slow_rel, 1)
                    dve.wait_ge(slow_win, n + 1)
                    dve.wait_ge(slow_added, n + 1)
                    add_window(k, w * WIN, slow_added)
                dve.wait_ge(slow_rel, g * NWIN + NWIN)
                select(g, k, [rel_slow[:, j:j + 1] for j in range(TILES)], sel_ready)
                dve.wait_ge(win_done, g + 1)
                dve.wait_ge(slow_added, (g + 1) * (NWIN - 1) + 1)
                add_window(k, NP - WIN, agg_added)

            def step(s, k, fits, q):
                edge = isinstance(s, int)
                mid = not edge or 0 <= s - 1 < NG
                end = not edge or 0 <= s - 2 < NG
                if end and fits:
                    start = dve.value_load(base_i[0:1, bass.ds(s - 2, 1)], min_val=0, max_val=N)
                if mid:
                    clamp2(s - 1, k - 1)
                if mid and fits:
                    select_own(s - 1, (k - 1) % UNROLL)
                if not edge or s + 1 < NG:
                    clamp1(s + 1, k + 1)
                if end and fits:
                    add_own(s - 2, (k - 2) % UNROLL, start)
                if mid:
                    filt(s - 1, k - 1)
                if not edge or s + 1 < NG:
                    act1(s + 1, k + 1)
                if mid:
                    message(s - 1, (k - 1) % UNROLL, q + (k - 1) // UNROLL)
                if end and not fits:
                    add_all(s - 2, (k - 2) % UNROLL)

            dve.wait_ge(cut_ready, 1)
            dve.wait_ge(windows_ready, 1)
            dve.wait_ge(slow_added, 1)
            widest_span = dve.value_load(widest_i[0:1, 0:1], min_val=0, max_val=NP)

            def edges(fits):
                for s in range(UNROLL):
                    step(s, s, fits, 0)
                with dve.Fori(1, NG // UNROLL - 1) as q:
                    for k in range(UNROLL):
                        step(q * UNROLL + k, k, fits, q)
                for s in range(NG - UNROLL, NG + 2):
                    step(s, s % UNROLL, fits, s // UNROLL)

            with dve.If(widest_span < WIN):
                edges(True)
            with dve.Else():
                edges(False)

            steps = [0]

            def then(ins):
                steps[0] += 1
                ins.then_inc(out_step, 1)
                dve.wait_ge(out_step, steps[0])

            def o_clamp(c):
                n = chunk_tiles(c) * P
                dve.wait_ge(oexp_done, c + 1)
                ev = e1[:, c % 2, :].rearrange("p (h n) -> p h n", h=KF)[:, :, 0:n]
                nc.vector.tensor_scalar(ev, ev, EXP_MAX, None, ALU.min).then_inc(oclamp_done, 1)

            def o_act(c):
                n = chunk_tiles(c) * P
                dve.wait_ge(oln_done, c + 1)
                if c >= 2:
                    dve.wait_ge(o2_done, c - 1)
                for h in range(KF):
                    last = nc.vector.scalar_tensor_tensor(
                        out=a1[:, c % 2, h * GE:h * GE + n], in0=u1[c % 2][:, h, 0:n], scalar=o1_bias_ln2[:, h:h + 1],
                        in1=e1[:, c % 2, h * GE:h * GE + n], op0=ALU.add, op1=ALU.max)
                last.then_inc(t_ready, 1)

            def o_sum(c):
                n = chunk_tiles(c)
                ts = slice(TILES * c, TILES * c + n)
                dve.wait_ge(o2_done, c + 1)
                nc.vector.tensor_tensor(z[:, ts, :].rearrange("p t f -> p (t f)"),
                                        u2[c % 2].rearrange("p a f -> p (a f)")[:, 0:n * F],
                                        z[:, ts, :].rearrange("p t f -> p (t f)"), ALU.add).then_inc(z_ready, 1)
                dve.wait_ge(z_ready, c + 1)
                for t in range(TILES * c, TILES * c + n):
                    last = nc.vector.bn_stats(stats[:, t, :], z[:, t, :])
                then(last)
                for t in range(TILES * c, TILES * c + n):
                    last = nc.vector.bn_aggr(mv[:, t, :], stats[:, t, :])
                then(last)
                nc.vector.tensor_scalar(var_eps[:, ts], mv[:, ts, 1], EPS, None, ALU.add).then_inc(var_ready, 1)

            def o_scale(c):
                ts = slice(TILES * c, TILES * c + chunk_tiles(c))
                dve.wait_ge(rstd0_ready, c + 1)
                then(nc.vector.tensor_tensor(newton[:, ts], rstd0[:, ts], rstd0[:, ts], ALU.mult))
                then(nc.vector.scalar_tensor_tensor(out=newton[:, ts], in0=newton[:, ts], scalar=-0.5,
                                                    in1=var_eps[:, ts], op0=ALU.mult, op1=ALU.mult))
                then(nc.vector.scalar_tensor_tensor(out=rstd[:, ts], in0=newton[:, ts], scalar=1.5,
                                                    in1=rstd0[:, ts], op0=ALU.add, op1=ALU.mult))
                nc.vector.scalar_tensor_tensor(out=shift[:, ts], in0=mv[:, ts, 0], scalar=-1.0,
                                               in1=rstd[:, ts], op0=ALU.mult, op1=ALU.mult).then_inc(scale_ready, 1)

            dve.wait_ge(xb_ready, 1)
            for c in range(CHUNKS + 2):
                if c < CHUNKS:
                    o_clamp(c)
                if c >= 2:
                    o_scale(c - 2)
                if c < CHUNKS:
                    o_act(c)
                if 1 <= c <= CHUNKS:
                    o_sum(c - 1)


_WEIGHTS = ['aw_W', 'aw_b', 'm1_W', 'm1_b', 'm2_W', 'm2_b', 'o1_W', 'o1_b', 'o2_W', 'o2_b']


def kernel(**inputs):
    import numpy as np
    import concourse.bacc as bacc
    from concourse import mybir as mb
    from concourse.bass_utils import run_bass_kernel_spmd

    x = np.asarray(inputs["x"])
    n, f = x.shape
    edges = inputs["src"].shape[0]
    attrs = inputs["edge_attr_50"].shape[1]
    nodes_pad = -(-n // P) * P
    edges_pad = -(-edges // (GE * UNROLL)) * GE * UNROLL
    rows = P // 2
    more = edges_pad - edges

    def by_tile(a, fill):
        a = np.pad(np.asarray(a), (0, more), constant_values=fill)
        return np.ascontiguousarray(a.reshape(-1, P).T)

    x_pad = np.pad(x, ((0, nodes_pad - n), (0, 0)))
    attr = np.zeros((rows, edges_pad), x.dtype)
    attr[:attrs, :edges] = np.asarray(inputs["edge_attr_50"]).T
    attr[attrs] = 1
    arrays = {
        "x": x_pad,
        "xT": np.ascontiguousarray(x_pad.T),
        "attrT": attr,
        "src": by_tile(inputs["src"], 0),
        "dst": by_tile(inputs["dst"], n),
        "dst_groups": np.pad(np.asarray(inputs["dst"]), (0, more), constant_values=n).reshape(-1, GE),
        "edge_weight": by_tile(inputs["edge_weight"], 0),
    }
    for w in _WEIGHTS:
        arrays[w] = np.ascontiguousarray(inputs["L0_gnn_" + w])
    arrays["o1_b"] = np.ascontiguousarray(arrays["o1_b"].reshape(-1, P).T)

    nc = bacc.Bacc("TRN2", target_bir_lowering=False, num_devices=1)
    args = {k: nc.dram_tensor(f"in_{k}", a.shape, mb.dt.from_np(a.dtype), kind="ExternalInput").ap()
            for k, a in arrays.items()}
    out = nc.dram_tensor("out_0", (n, f), mb.dt.float32, kind="ExternalOutput").ap()
    gnn_resnorm_kernel(nc, **args, out=out)
    r = run_bass_kernel_spmd(nc, [{f"in_{k}": a for k, a in arrays.items()}], core_ids=[0])
    return r.results[0]["out_0"]
```

```python
from contextlib import ExitStack
import math

import concourse.bass as bass
from concourse import mybir

F32 = mybir.dt.float32
BF16 = mybir.dt.bfloat16
I32 = mybir.dt.int32
F32R = mybir.dt.float32r
ALU = mybir.AluOpType
ACT = mybir.ActivationFunctionType
AX = mybir.AxisListType.X

P = 128
TILES = 4
GE = TILES * P
WIN = 64
UNROLL = 4
LN2 = math.log(2.0)
EXP_MAX = 2.0 ** 60
CUTOFF = 10.0
EPS = 1e-5
LN_EXP_TABLE = 6


def positive(count):
    return not isinstance(count, int) or count > 0


def gnn_resnorm_kernel(nc, x, xT, attrT, src, dst, dst_groups, edge_weight,
                       aw_W, aw_b, m1_W, m1_b, m2_W, m2_b, o1_W, o1_b, o2_W, o2_b, out):
    N, F = out.shape
    NP = x.shape[0]
    NTILES = NP // P
    AR = attrT.shape[0]
    G = m1_W.shape[0]
    KF = F // P
    NT = src.shape[1]
    NG = NT // TILES
    NWIN = NP // WIN
    UNITS = (NTILES + 1) // 2
    H1_BEFORE_M1 = UNITS - 5
    CHUNKS = (NTILES + TILES - 1) // TILES
    assert KF == 2 and NG % UNROLL == 0 and N + WIN <= NP + WIN and NWIN * WIN == NP

    with ExitStack() as ctx:
        def sb(name, shape, dt=F32):
            return ctx.enter_context(nc.sbuf_tensor(name, shape, dt))

        def sem(name):
            return ctx.enter_context(nc.semaphore(name))

        psum = ctx.enter_context(nc.psum_tensor("psum", [P, 8, 512], F32))
        u1 = [psum[:, 2 * b:2 * b + 2, :] for b in range(2)]
        u2 = [psum[:, 4 + 2 * b:6 + 2 * b, :] for b in range(2)]
        win_sum = [psum[:, 2 * b, 0:KF * WIN].rearrange("p (k n) -> p k n", k=KF) for b in range(2)]
        last_sum = psum[:, 2 * ((NG - 1) % 2):2 * ((NG - 1) % 2) + 2, 0:WIN]
        lo_bc, hi_bc = psum[:, 2, 0:NG], psum[:, 3, 0:NG]

        h1_table = nc.dram_tensor("h1_table", (NP, F), F32, kind="Internal").ap()

        aw_sb = sb("aw_sb", [P, KF, F])
        m1_sb = sb("m1_sb", [P, F])
        m1_part = sb("m1_part", [P, 2, F], F32R)
        m2_sb = sb("m2_sb", [P, KF, F])
        o1_sb = sb("o1_sb", [P, KF, F])
        o2_sb = sb("o2_sb", [P, KF, F])
        aw_bias = sb("aw_bias", [P, F])
        o2_bias = sb("o2_bias", [P, F])
        o1_bias = sb("o1_bias", [P, KF])
        o1_bias_ln2 = sb("o1_bias_ln2", [P, KF])
        m2_bias = sb("m2_bias", [P, F])
        m2_rest = sb("m2_rest", [P, 2, F])
        m2_part = sb("m2_part", [P, 3, F], BF16)
        m2_bias_rows = sb("m2_bias_rows", [P, 2, F], BF16)
        ones_bf = sb("ones_bf", [P, P], BF16)
        src_sb = sb("src_sb", [P, NT], I32)
        dst_sb = sb("dst_sb", [P, NT], I32)
        rel = sb("rel", [P, NT])
        cut = sb("cut", [P, NT])
        turns = sb("turns", [P, NT], I32)
        dst_g = sb("dst_g", [NG, GE], I32)
        ident = sb("ident", [P, P])
        iota_i = sb("iota_i", [P, WIN], I32)
        iota = sb("iota", [P, WIN])
        span_ends = sb("span_ends", [NG, 2])
        ends_wide = sb("ends_wide", [NG, 2, P])
        base = sb("base", [P, NG])
        span = sb("span", [P, NG])
        widest = sb("widest", [P, 1])
        base_i = sb("base_i", [P, NG], I32)
        widest_i = sb("widest_i", [P, 1], I32)
        rel_slow = sb("rel_slow", [P, TILES])
        att = sb("att", [P, 2, 2 * GE])
        att_part = sb("att_part", [P, 2, 2 * GE], F32R)
        e1 = sb("e1", [P, 2, KF * GE])
        a1 = sb("a1", [P, 2, KF * GE])
        e2 = sb("e2", [P, 2, TILES * F])
        msg = sb("msg", [P, 4, TILES * F])
        idx_now = sb("idx_now", [P, 4, TILES], I32)
        sel = sb("sel", [P, 2, TILES, WIN])
        agg = sb("agg", [P, KF, NP + WIN])
        xT_sb = sb("xT_sb", [P, KF, NP])
        h1_sb = sb("h1_sb", [P, NTILES, F])
        z = sb("z", [P, NTILES, F])
        stats = sb("stats", [P, NTILES, 6])
        mv = sb("mv", [P, NTILES, 2])
        var_eps = sb("var_eps", [P, NTILES])
        rstd0 = sb("rstd0", [P, NTILES])
        rstd = sb("rstd", [P, NTILES])
        newton = sb("newton", [P, NTILES])
        shift = sb("shift", [P, NTILES])
        half_pi = sb("half_pi", [P, 1])
        half_one = sb("half_one", [P, 1])

        dst_loaded = sem("dst_loaded")
        edge_loaded = sem("edge_loaded")
        bias_loaded = sem("bias_loaded")
        m1_loaded = sem("m1_loaded")
        m2_loaded = sem("m2_loaded")
        aw_loaded = sem("aw_loaded")
        o_loaded = sem("o_loaded")
        XT_CUTS = [0, 512, 1024, 2048, NP]
        xT_loaded = [sem(f"xT_loaded{i}") for i in range(4)]
        x_loaded = sem("x_loaded")
        att_loaded = [sem(f"att_loaded{i}") for i in range(2)]
        consts_ready = sem("consts_ready")
        zeros_ready = sem("zeros_ready")
        setup_step = sem("setup_step")
        ends_ready = sem("ends_ready")
        ends_spread = sem("ends_spread")
        windows_ready = sem("windows_ready")
        m1_ready = sem("m1_ready")
        m2_bias_ready = sem("m2_bias_ready")
        turns_ready = sem("turns_ready")
        sin_done = sem("sin_done")
        cut_ready = sem("cut_ready")
        h1_done = sem("h1_done")
        h1_ready = sem("h1_ready")
        h1_stored = sem("h1_stored")
        xb_ready = sem("xb_ready")
        att_rounded = sem("att_rounded")
        att_ready = sem("att_ready")
        m1_done = sem("m1_done")
        exp1_done = sem("exp1_done")
        clamp1_done = sem("clamp1_done")
        ln1_done = sem("ln1_done")
        a1_ready = sem("a1_ready")
        bias_laid = sem("bias_laid")
        m2_done = sem("m2_done")
        exp2_done = sem("exp2_done")
        clamp2_done = sem("clamp2_done")
        ln2_done = sem("ln2_done")
        wf_ready = sem("wf_ready")
        idx_ready = sem("idx_ready")
        gathered = [sem(f"gathered{i}") for i in range(4)]
        msg_ready = sem("msg_ready")
        sel_ready = sem("sel_ready")
        win_done = sem("win_done")
        agg_added = sem("agg_added")
        slow_rel = sem("slow_rel")
        slow_sel = sem("slow_sel")
        slow_win = sem("slow_win")
        slow_added = sem("slow_added")
        o1_done = sem("o1_done")
        oexp_done = sem("oexp_done")
        oclamp_done = sem("oclamp_done")
        oln_done = sem("oln_done")
        t_ready = sem("t_ready")
        o2_done = sem("o2_done")
        out_step = sem("out_step")
        z_ready = sem("z_ready")
        var_ready = sem("var_ready")
        lnv_done = sem("lnv_done")
        rstd0_ready = sem("rstd0_ready")
        scale_ready = sem("scale_ready")
        y_ready = sem("y_ready")
        stored = sem("stored")

        block = ctx.enter_context(nc.Block())

        rest = NTILES - TILES * (CHUNKS - 2)

        def first_tile(c):
            return 0 if c == 0 else (rest + 1) // 2 + TILES * (c - 1)

        def chunk_tiles(c):
            return (rest + 1) // 2 if c == 0 else rest // 2 if c == CHUNKS - 1 else TILES

        def count(g, half):
            return g + 1 + (half or 0)

        def part(columns, half):
            return columns if half is None else columns[:, half * 2 * F:(half + 1) * 2 * F]

        def u2_part(b, half):
            return u2[b] if half is None else u2[b][:, half, :]

        @block.sync
        def _(sp):
            sp.dma_start(aw_sb[:, :, :], aw_W.rearrange("(k p) f -> p k f", p=P)).then_inc(aw_loaded, 16)
            xT_v = xT.rearrange("(k p) n -> p k n", p=P)
            for i in range(4):
                a, b = XT_CUTS[i], XT_CUTS[i + 1]
                sp.dma_start(xT_sb[:, :, a:b], xT_v[:, :, a:b]).then_inc(xT_loaded[i], 16)
                if i == 0:
                    sp.dma_start(dst_g[:, :], dst_groups).then_inc(dst_loaded, 16)
                    sp.dma_start(dst_sb[:, :], dst).then_inc(edge_loaded, 16)
                    sp.dma_start(cut[:, :], edge_weight).then_inc(edge_loaded, 16)
                    sp.dma_start(src_sb[:, :], src).then_inc(edge_loaded, 16)
                    sp.dma_start(aw_bias[:, :], aw_b.partition_broadcast(P)).then_inc(bias_loaded, 16)
                    sp.dma_start(m2_bias[:, :], m2_b.partition_broadcast(P)).then_inc(bias_loaded, 16)
                    sp.dma_start(o2_bias[:, :], o2_b.partition_broadcast(P)).then_inc(bias_loaded, 16)
                    sp.dma_start(o1_bias[:, :], o1_b).then_inc(bias_loaded, 16)
                if i == 1:
                    sp.wait_ge(zeros_ready, 1)
                    for r in (0, AR):
                        sp.dma_start(m1_sb[r:r + G, :], m1_W).then_inc(m1_loaded, 16)
                        sp.dma_start(m1_sb[r + G:r + G + 1, :], m1_b.rearrange("(a f) -> a f", a=1))\
                          .then_inc(m1_loaded, 16)
            for c in range(2):
                for r in range(2):
                    sp.dma_start(att[r * AR:(r + 1) * AR, c, :], attrT[:, c * 2 * GE:(c + 1) * 2 * GE])\
                      .then_inc(att_loaded[c], 16)
            sp.dma_start(m2_sb[:, :, :], m2_W.rearrange("(k p) f -> p k f", p=P)).then_inc(m2_loaded, 16)
            for u in range(UNITS):
                n = min(2, NTILES - 2 * u)
                sp.wait_ge(h1_ready, u + 1)
                sp.dma_start(h1_table[u * 2 * P:(u * 2 + n) * P, :].rearrange("(t p) f -> p t f", p=P),
                             h1_sb[:, 2 * u:2 * u + n, :]).then_inc(h1_stored, 16)
            def attributes(q, k):
                sp.wait_ge(att_ready, q * 2 + (k - 1))
                for r in range(2):
                    sp.dma_start(att[r * AR:(r + 1) * AR, k, :], attrT[:, bass.ds((q * 2 + k) * 2 * GE, 2 * GE)])\
                      .then_inc(att_loaded[k], 16)

            for q in range(1, 4):
                for k in range(2):
                    attributes(q, k)
            sp.dma_start(z[:, :, :], x.rearrange("(t p) f -> p t f", p=P)).then_inc(x_loaded, 16)
            sp.dma_start(o1_sb[:, :, :], o1_W.rearrange("(k p) f -> p k f", p=P)).then_inc(o_loaded, 16)
            sp.dma_start(o2_sb[:, :, :], o2_W.rearrange("(k p) f -> p k f", p=P)).then_inc(o_loaded, 16)
            with sp.Fori(4, NG // UNROLL) as q:
                for k in range(2):
                    attributes(q, k)
            stores = 0
            for c in range(CHUNKS):
                sp.wait_ge(y_ready, c + 1)
                t0, n = first_tile(c), chunk_tiles(c)
                full = min(n, N // P - t0)
                if full > 0:
                    sp.dma_start(out[t0 * P:(t0 + full) * P, :].rearrange("(t p) f -> p t f", p=P),
                                 z[:, t0:t0 + full, :]).then_inc(stored, 16)
                    stores += 1
                if full < n:
                    sp.dma_start(out[N // P * P:N, :], z[0:N % P, N // P, :]).then_inc(stored, 16)
                    stores += 1
            sp.wait_ge(stored, 16 * stores)

        @block.gpsimd
        def _(pool):
            pool.memset(ident[:, :], 0.0).then_inc(consts_ready, 1)
            pool.wait_ge(consts_ready, 1)
            pool.affine_select(out=ident[:, :], in_=ident[:, :], compare_op=ALU.not_equal, fill=1.0, base=0,
                               pattern=[[-1, P]], channel_multiplier=1).then_inc(consts_ready, 1)
            pool.iota(iota_i[:, :], [[1, WIN]], base=0, channel_multiplier=0).then_inc(consts_ready, 1)
            nc.gpsimd.memset(agg[:, :, :], 0.0).then_inc(slow_added, 1)
            pool.wait_ge(edge_loaded, 48)

            def copy_indices(g, k):
                pool.tensor_copy(idx_now[:, k, :], src_sb[:, bass.ds(g * TILES, TILES)]).then_inc(idx_ready, 1)

            def gather(g, k, q, last=False):
                if positive(g - 3):
                    pool.wait_ge(win_done, g - 3)
                if not last and positive(q + k // 3):
                    pool.wait_ge(gathered[(k + 1) % 4], q * (16 * TILES) + k // 3 * 16 * TILES)
                pool.wait_ge(idx_ready, g + 1)
                if not last:
                    copy_indices(g + 1, (k + 1) % 4)
                for j in range(TILES):
                    pool.indirect_dma_start(msg[:, k, j * F:(j + 1) * F], None, h1_table,
                                            bass.IndirectOffsetOnAxis(idx_now[:, k, j:j + 1], 0))\
                        .then_inc(gathered[k], 16)

            def low_parts(c, slot):
                low = slice(0, AR)
                pool.wait_ge(att_rounded, c + 1)
                pool.tensor_tensor(att_part[low, slot, :], att[low, slot, :], att_part[low, slot, :].bitcast(F32),
                                   ALU.subtract).then_inc(att_ready, 1)

            low_parts(0, 0)
            low_parts(1, 1)
            copy_indices(0, 0)
            pool.wait_ge(h1_stored, 16 * UNITS)
            for k in range(4):
                gather(k, k, 0)
                if k == 1:
                    low_parts(2, 0)
            with pool.Fori(1, NG // UNROLL - 1) as q:
                for k in range(4):
                    gather(q * UNROLL + k, k, q)
                    if k % 2 == 0:
                        low_parts(q * 2 + 1 + k // 2, (k // 2 + 1) % 2)
            for k in range(4):
                gather(NG - UNROLL + k, k, NG // UNROLL - 1, last=(k == 3))
                if k == 0:
                    low_parts(NG // 2 - 1, 1)
            pool.wait_ge(x_loaded, 16)
            pool.wait_ge(bias_loaded, 64)
            for t in range(NTILES):
                last = pool.tensor_tensor(z[:, t, :], z[:, t, :], o2_bias[:, :], ALU.add)
            last.then_inc(xb_ready, 1)

        @block.scalar
        def _(act):
            act.wait_ge(turns_ready, 1)
            nc.scalar.activation(cut[:, :], cut[:, :], ACT.Abs).then_inc(sin_done, 1)
            act.wait_ge(sin_done, 1)
            nc.scalar.activation(cut[:, :], cut[:, :], ACT.Sin, bias=half_pi[:, 0:1],
                                 scale=-math.pi / (2 * CUTOFF)).then_inc(sin_done, 1)
            act.add_instruction(mybir.InstLoadActFuncSet(name=nc.get_next_instruction_name(),
                                                         act_func_set_id=LN_EXP_TABLE, ins=[], outs=[]))

            def round_attributes(c, slot, rounds):
                act.wait_ge(att_loaded[slot], 32 * rounds + 32)
                if positive(c - 1):
                    act.wait_ge(m1_done, c * 2 - 2)
                nc.scalar.activation(att_part[:, slot, :], att[:, slot, :], ACT.Copy).then_inc(att_rounded, 1)

            def exp1(g, k):
                b = k % 2
                act.wait_ge(m1_done, g + 1)
                if positive(g - 1):
                    act.wait_ge(a1_ready, g - 1)
                nc.scalar.activation(e1[:, b, :], u1[b], ACT.Exp).then_inc(exp1_done, 1)

            def ln1(g, k):
                b = k % 2
                act.wait_ge(clamp1_done, g + 1)
                nc.scalar.activation(e1[:, b, :], e1[:, b, :], ACT.Ln, bias=half_one[:, 0:1], scale=0.5)\
                  .then_inc(ln1_done, 1)

            def exp2(g, k, half=None):
                b = k % 2
                act.wait_ge(m2_done, count(g, half))
                if positive(g - 1):
                    act.wait_ge(msg_ready, g - 1)
                nc.scalar.activation(part(e2[:, b, :], half), u2_part(b, half), ACT.Exp).then_inc(exp2_done, 1)

            def lay_bias(g, k):
                act.wait_ge(wf_ready, g - 1)
                nc.scalar.activation(u2[k % 2].rearrange("p a (t f) -> p (a t) f", f=F),
                                     m2_bias[:, :].unsqueeze(1).to_broadcast([P, TILES, F]), ACT.Copy)\
                  .then_inc(bias_laid, 1)

            def ln2(g, k, half=None):
                b = k % 2
                act.wait_ge(clamp2_done, count(g, half))
                nc.scalar.activation(part(e2[:, b, :], half), part(e2[:, b, :], half), ACT.Ln, bias=half_one[:, 0:1],
                                     scale=0.5).then_inc(ln2_done, 1)

            def step(s, k, q):
                edge = isinstance(s, int)
                if not edge or 0 <= s - 1 < NG:
                    exp2(s - 1, k - 1)
                if not edge or s + 1 < NG:
                    exp1(s + 1, k + 1)
                if not edge or 0 <= s - 1 < NG:
                    ln2(s - 1, k - 1)
                if not edge or s + 1 < NG:
                    ln1(s + 1, k + 1)
                if not edge or 2 <= s + 1 < NG:
                    lay_bias(s + 1, k + 1)
                if k % 2 == 0 and (not edge or s + 4 < NG):
                    round_attributes(q * 2 + 2 + k // 2, k // 2, q + 1)

            for c in range(2):
                round_attributes(c, c, 0)
            exp1(0, 0)
            ln1(0, 0)
            for s in range(UNROLL):
                step(s, s, 0)
            with act.Fori(1, NG // UNROLL - 1) as q:
                for k in range(UNROLL):
                    step(q * UNROLL + k, k, q)
            for s in range(NG - UNROLL, NG):
                step(s, s % UNROLL, s // UNROLL)
            for half in range(2):
                exp2(NG - 1, NG - 1, half)
            for half in range(2):
                ln2(NG - 1, NG - 1, half)

            def o_exp(c):
                n = chunk_tiles(c) * P
                act.wait_ge(o1_done, c + 1)
                if c >= 2:
                    act.wait_ge(t_ready, c - 1)
                for h in range(KF):
                    last = nc.scalar.activation(e1[:, c % 2, h * GE:h * GE + n], u1[c % 2][:, h, 0:n], ACT.Exp,
                                                bias=o1_bias[:, h:h + 1])
                    if h == KF - 1:
                        last.then_inc(oexp_done, 1)

            def o_ln(c):
                n = chunk_tiles(c) * P
                act.wait_ge(oclamp_done, c + 1)
                ev = e1[:, c % 2, :].rearrange("p (h n) -> p h n", h=KF)[:, :, 0:n]
                nc.scalar.activation(ev, ev, ACT.Ln, bias=half_one[:, 0:1], scale=0.5).then_inc(oln_done, 1)

            def o_rstd(c):
                ts = slice(first_tile(c), first_tile(c) + chunk_tiles(c))
                act.wait_ge(var_ready, c + 1)
                nc.scalar.activation(rstd0[:, ts], var_eps[:, ts], ACT.Ln).then_inc(lnv_done, 1)
                act.wait_ge(lnv_done, c + 1)
                nc.scalar.activation(rstd0[:, ts], rstd0[:, ts], ACT.Exp, scale=-0.5).then_inc(rstd0_ready, 1)

            def o_norm(c):
                act.wait_ge(scale_ready, c + 1)
                for t in range(first_tile(c), first_tile(c) + chunk_tiles(c)):
                    last = nc.scalar.activation(z[:, t, :], z[:, t, :], ACT.Identity, bias=shift[:, t:t + 1],
                                                scale=rstd[:, t:t + 1])
                    if t == first_tile(c) + chunk_tiles(c) - 1:
                        last.then_inc(y_ready, 1)

            act.wait_ge(bias_loaded, 64)
            for c in range(CHUNKS + 2):
                if c < CHUNKS:
                    o_exp(c)
                if c >= 2:
                    o_rstd(c - 2)
                if c < CHUNKS:
                    o_ln(c)
                if c >= 2:
                    o_norm(c - 2)

        @block.tensor
        def _(pe):
            def h1(u):
                n = min(2, NTILES - 2 * u)
                if 2 * u * P in XT_CUTS:
                    pe.wait_ge(xT_loaded[XT_CUTS.index(2 * u * P)], 16)
                if u >= 4:
                    pe.wait_ge(h1_ready, u - 3)
                bank = psum[:, 4 + u % 4, :]
                for j in range(n):
                    t = 2 * u + j
                    for kf in range(KF):
                        last = nc.tensor.matmul(bank[:, j * F:(j + 1) * F], xT_sb[:, kf, t * P:(t + 1) * P],
                                                aw_sb[:, kf, :], start=(kf == 0), stop=(kf == KF - 1))
                last.then_inc(h1_done, 1)

            def m1(g, k, c):
                b = k % 2
                pe.wait_ge(att_ready, c * 2 + k // 2 + 1)
                if positive(g - 3):
                    pe.wait_ge(agg_added, g - 3)
                for h in range(KF):
                    for part in range(2):
                        last = nc.tensor.matmul(u1[b][:, h, :], m1_part[:, part, h * P:(h + 1) * P],
                                                att_part[:, k // 2, k % 2 * GE:(k % 2 + 1) * GE],
                                                start=(part == 0), stop=(part == 1))
                last.then_inc(m1_done, 1)

            def m2(g, k, h, halves):
                b = k % 2
                opens = isinstance(g, int) and g < 2
                if h == 0:
                    pe.wait_ge(a1_ready, g + 1)
                    if not opens:
                        pe.wait_ge(bias_laid, g - 1)
                if opens:
                    nc.tensor.matmul(u2[b][:, h, :], ones_bf[:, :], m2_bias_rows[:, :, :].rearrange("p a f -> p (a f)"),
                                     start=True, stop=False, skip_group_check=True)
                for j in range(2):
                    for kf in range(KF):
                        e0 = kf * GE + (2 * h + j) * P
                        last = nc.tensor.matmul(u2[b][:, h, j * F:(j + 1) * F], a1[:, b, e0:e0 + P],
                                                m2_sb[:, kf, :], start=False, stop=(kf == KF - 1),
                                                skip_group_check=True)
                if h == 1 or halves:
                    last.then_inc(m2_done, 1)

            def window(k, signal):
                for h in range(KF):
                    for j in range(TILES):
                        last = nc.tensor.matmul(win_sum[k % 2][:, h, :], msg[:, k, j * F + h * P:j * F + (h + 1) * P],
                                                sel[:, k % 2, j, :], start=(j == 0), stop=(j == TILES - 1))
                last.then_inc(signal, 1)

            def window_halves(k):
                for half in range(2):
                    pe.wait_ge(msg_ready, count(NG - 1, half))
                    for h in range(KF):
                        for j in (2 * half, 2 * half + 1):
                            last = nc.tensor.matmul(last_sum[:, h, :],
                                                    msg[:, k, j * F + h * P:j * F + (h + 1) * P],
                                                    sel[:, k % 2, j, :], start=(j == 0), stop=(j == TILES - 1))
                last.then_inc(win_done, 1)

            def scatter(g, k, fits, halves, u1_busy):
                def enter():
                    pe.wait_ge(msg_ready, g + 2 if halves else g + 1)
                    if u1_busy:
                        pe.wait_ge(a1_ready, g + 3)

                if not fits:
                    with pe.Fori(0, NWIN - 1) as w:
                        enter()
                        n = g * (NWIN - 1) + w
                        pe.wait_ge(slow_sel, n + 1)
                        pe.wait_ge(slow_added, n + 1)
                        window(k, slow_win)
                    pe.wait_ge(slow_added, (g + 1) * (NWIN - 1) + 1)
                if halves and fits:
                    pe.wait_ge(sel_ready, g + 1)
                    window_halves(k)
                else:
                    enter()
                    pe.wait_ge(sel_ready, g + 1)
                    window(k, win_done)

            def step(s, k, fits, q):
                edge = isinstance(s, int)
                if not edge or s < NG:
                    m2(s, k, 0, halves=edge and s == NG - 1)
                if not edge or 0 <= s - 2 < NG:
                    scatter(s - 2, (k - 2) % UNROLL, fits, halves=edge and s - 2 == NG - 1,
                            u1_busy=not edge or s < NG)
                if not edge or s < NG:
                    m2(s, k, 1, halves=edge and s == NG - 1)
                if not edge or s + 2 < NG:
                    m1(s + 2, (k + 2) % UNROLL, q + (k + 2) // UNROLL)

            pe.wait_ge(aw_loaded, 16)
            for u in range(2):
                h1(u)
            pe.wait_ge(consts_ready, 2)
            pe.wait_ge(ends_ready, 1)
            for e, spread in enumerate((lo_bc, hi_bc)):
                last = nc.tensor.matmul(spread, ends_wide[:, e, :], ident[0:NG, 0:NG], start=True, stop=True)
            last.then_inc(ends_spread, 1)
            for u in range(2, H1_BEFORE_M1):
                h1(u)
            pe.wait_ge(m1_ready, 1)
            pe.wait_ge(windows_ready, 1)
            m1(0, 0, 0)
            m1(1, 1, 0)
            for u in range(H1_BEFORE_M1, UNITS):
                h1(u)
            pe.wait_ge(m2_loaded, 16)
            pe.wait_ge(m2_bias_ready, 1)
            pe.wait_ge(h1_ready, UNITS)
            widest_span = pe.value_load(widest_i[0:1, 0:1], min_val=0, max_val=NP)

            def edges(fits):
                for s in range(UNROLL):
                    step(s, s, fits, 0)
                with pe.Fori(1, NG // UNROLL - 1) as q:
                    for k in range(UNROLL):
                        step(q * UNROLL + k, k, fits, q)
                for s in range(NG - UNROLL, NG + 2):
                    step(s, s % UNROLL, fits, s // UNROLL)

            with pe.If(widest_span < WIN):
                edges(True)
            with pe.Else():
                edges(False)

            def o1(c):
                n = chunk_tiles(c) * P
                if c >= 2:
                    pe.wait_ge(t_ready, c - 1)
                for h in range(KF):
                    for kf in range(KF):
                        last = nc.tensor.matmul(u1[c % 2][:, h, 0:n], o1_sb[:, kf, h * P:(h + 1) * P],
                                                agg[:, kf, first_tile(c) * P:first_tile(c) * P + n],
                                                start=(kf == 0), stop=(kf == KF - 1))
                last.then_inc(o1_done, 1)

            def o2(c):
                pe.wait_ge(t_ready, c + 1)
                if c >= 2:
                    pe.wait_ge(z_ready, c - 1)
                for j in range(chunk_tiles(c)):
                    for kf in range(KF):
                        e0 = kf * GE + j * P
                        last = nc.tensor.matmul(u2[c % 2][:, j // 2, j % 2 * F:(j % 2 + 1) * F], a1[:, c % 2, e0:e0 + P],
                                                o2_sb[:, kf, :], start=(kf == 0), stop=(kf == KF - 1))
                last.then_inc(o2_done, 1)

            pe.wait_ge(o_loaded, 32)
            pe.wait_ge(agg_added, NG)
            o1(0)
            for c in range(CHUNKS):
                if c + 1 < CHUNKS:
                    o1(c + 1)
                o2(c)

        @block.vector
        def _(dve):
            done = [0]

            def link(ins):
                done[0] += 1
                ins.then_inc(setup_step, 1)
                dve.wait_ge(setup_step, done[0])

            nc.vector.memset(m1_sb[:, :], 0.0).then_inc(zeros_ready, 1)
            nc.vector.memset(half_pi[:, :], math.pi / 2)
            nc.vector.memset(half_one[:, :], 0.5)
            nc.vector.memset(ones_bf[:, :], 1.0)
            link(nc.vector.memset(ends_wide[:, :, :], 1.0))

            dve.wait_ge(dst_loaded, 16)
            nc.vector.tensor_reduce(span_ends[:, 0:1], dst_g[:, :], AX, ALU.min)
            link(nc.vector.tensor_reduce(span_ends[:, 1:2], dst_g[:, :], AX, ALU.max))
            for e in range(2):
                last = nc.vector.tensor_scalar(ends_wide[:, e, :], ends_wide[:, e, :], span_ends[:, e:e + 1], None, ALU.mult)
            last.then_inc(ends_ready, 1)
            dve.wait_ge(consts_ready, 3)
            nc.vector.tensor_copy(iota[:, :], iota_i[:, :])
            dve.wait_ge(edge_loaded, 48)
            link(nc.vector.tensor_scalar(turns[:, :], cut[:, :], 1.0 / (2 * CUTOFF), None, ALU.mult))
            nc.vector.scalar_tensor_tensor(out=cut[:, :], in0=turns[:, :], scalar=-2 * CUTOFF, in1=cut[:, :],
                                           op0=ALU.mult, op1=ALU.add).then_inc(turns_ready, 1)
            dve.wait_ge(ends_spread, 1)
            link(nc.vector.tensor_copy(base[:, :], lo_bc))
            link(nc.vector.tensor_tensor(span[:, :], hi_bc, base[:, :], ALU.subtract))
            link(nc.vector.tensor_reduce(widest[:, :], span[:, :], AX, ALU.max))
            nc.vector.tensor_copy(base_i[:, :], base[:, :])
            link(nc.vector.tensor_copy(widest_i[:, :], widest[:, :]))
            rel_v = rel[:, :].rearrange("p (g j) -> p g j", j=TILES)
            dst_v = dst_sb[:, :].rearrange("p (g j) -> p g j", j=TILES)
            for j in range(TILES):
                last = nc.vector.tensor_tensor(rel_v[:, :, j], dst_v[:, :, j], base[:, :], ALU.subtract)
            last.then_inc(windows_ready, 1)

            def m1_parts():
                dve.wait_ge(m1_loaded, 64)
                link(nc.vector.tensor_copy(m1_part[:, 0, :], m1_sb[:, :]))
                nc.vector.tensor_tensor(m1_part[:, 1, :], m1_sb[:, :], m1_part[:, 0, :].bitcast(F32), ALU.subtract)\
                  .then_inc(m1_ready, 1)

            def m2_bias_parts():
                link(nc.vector.tensor_copy(m2_part[:, 0, :], m2_bias[:, :]))
                link(nc.vector.tensor_tensor(m2_rest[:, 0, :], m2_bias[:, :], m2_part[:, 0, :], ALU.subtract))
                link(nc.vector.tensor_copy(m2_part[:, 1, :], m2_rest[:, 0, :]))

            def m2_bias_last_part():
                link(nc.vector.tensor_tensor(m2_rest[:, 1, :], m2_rest[:, 0, :], m2_part[:, 1, :], ALU.subtract))
                nc.vector.memset(m2_bias_rows[:, :, :], 0.0)
                link(nc.vector.tensor_copy(m2_part[:, 2, :], m2_rest[:, 1, :]))

            def m2_bias_to_rows():
                for i in range(3):
                    for twice in range(2):
                        last = nc.vector.tensor_copy(m2_bias_rows[32 * i:32 * i + 1, twice, :],
                                                     m2_part[32 * i:32 * i + 1, i, :])
                last.then_inc(m2_bias_ready, 1)

            def square_cosine():
                dve.wait_ge(sin_done, 2)
                nc.vector.tensor_tensor(cut[:, :], cut[:, :], cut[:, :], ALU.mult).then_inc(cut_ready, 1)
                nc.vector.tensor_scalar(o1_bias_ln2[:, :], o1_bias[:, :], -LN2, None, ALU.add)

            def clamp1(g, k):
                b = k % 2
                dve.wait_ge(exp1_done, g + 1)
                nc.vector.tensor_scalar(e1[:, b, :], e1[:, b, :], EXP_MAX, None, ALU.min).then_inc(clamp1_done, 1)

            def act1(g, k):
                b = k % 2
                dve.wait_ge(ln1_done, g + 1)
                if positive(g - 1):
                    dve.wait_ge(m2_done, g - 1)
                nc.vector.scalar_tensor_tensor(out=a1[:, b, :].rearrange("p (h e) -> p h e", h=KF), in0=u1[b],
                                               scalar=-LN2, in1=e1[:, b, :].rearrange("p (h e) -> p h e", h=KF),
                                               op0=ALU.add, op1=ALU.max).then_inc(a1_ready, 1)

            between = {1: m1_parts, 3: m2_bias_parts, 4: m2_bias_last_part, 5: m2_bias_to_rows, 6: square_cosine,
                       H1_BEFORE_M1 + 1: lambda: clamp1(0, 0), H1_BEFORE_M1 + 2: lambda: act1(0, 0)}
            dve.wait_ge(bias_loaded, 64)
            for u in range(UNITS):
                n = min(2, NTILES - 2 * u)
                dve.wait_ge(h1_done, u + 1)
                nc.vector.tensor_tensor(h1_sb[:, 2 * u:2 * u + n, :],
                                        psum[:, 4 + u % 4, 0:n * F].rearrange("p (t f) -> p t f", t=n),
                                        aw_bias[:, :].unsqueeze(1).to_broadcast([P, n, F]), ALU.add).then_inc(h1_ready, 1)
                if u in between:
                    between[u]()

            def clamp2(g, k, half=None):
                dve.wait_ge(exp2_done, count(g, half))
                e = part(e2[:, k % 2, :], half)
                nc.vector.tensor_scalar(e, e, EXP_MAX, None, ALU.min).then_inc(clamp2_done, 1)

            def filt(g, k, half=None):
                b = k % 2
                dve.wait_ge(ln2_done, count(g, half))
                e = part(e2[:, b, :], half)
                if half is None:
                    e = e.rearrange("p (h e) -> p h e", h=2)
                nc.vector.scalar_tensor_tensor(out=e, in0=u2_part(b, half), scalar=-LN2, in1=e,
                                               op0=ALU.add, op1=ALU.max).then_inc(wf_ready, 1)

            def message(g, k, rounds, half=None):
                dve.wait_ge(gathered[k], rounds * (16 * TILES) + 16 * TILES)
                dve.wait_ge(wf_ready, count(g, half))
                rows = part(msg[:, k, :], half)
                nc.vector.tensor_tensor(rows, part(e2[:, k % 2, :], half), rows, ALU.mult).then_inc(msg_ready, 1)

            def select(g, k, rels, signal):
                for j in range(TILES):
                    last = nc.vector.tensor_scalar(sel[:, k % 2, j, :], iota[:, :], rels[j],
                                                   cut[:, bass.ds(g * TILES + j, 1)], ALU.is_equal, ALU.mult)
                last.then_inc(signal, 1)

            def add_window(sums, start, signal):
                nc.vector.tensor_tensor(agg[:, :, bass.ds(start, WIN)], agg[:, :, bass.ds(start, WIN)],
                                        sums, ALU.add).then_inc(signal, 1)

            def select_own(g, k):
                if positive(g - 1):
                    dve.wait_ge(win_done, g - 1)
                select(g, k, [rel[:, bass.ds(g * TILES + j, 1)] for j in range(TILES)], sel_ready)

            def add_own(g, sums, start):
                dve.wait_ge(win_done, g + 1)
                if positive(g):
                    dve.wait_ge(agg_added, g)
                add_window(sums, start, agg_added)

            def add_all(g, k):
                if positive(g):
                    dve.wait_ge(sel_ready, g)
                nc.vector.tensor_copy(rel_slow[:, :], dst_sb[:, bass.ds(g * TILES, TILES)]).then_inc(slow_rel, 1)
                with dve.Fori(0, NWIN - 1) as w:
                    n = g * (NWIN - 1) + w
                    dve.wait_ge(slow_rel, g * NWIN + w + 1)
                    select(g, k, [rel_slow[:, j:j + 1] for j in range(TILES)], slow_sel)
                    dve.wait_ge(slow_sel, n + 1)
                    nc.vector.tensor_scalar(rel_slow[:, :], rel_slow[:, :], -float(WIN), None, ALU.add)\
                      .then_inc(slow_rel, 1)
                    dve.wait_ge(slow_win, n + 1)
                    dve.wait_ge(slow_added, n + 1)
                    add_window(win_sum[k % 2], w * WIN, slow_added)
                dve.wait_ge(slow_rel, g * NWIN + NWIN)
                select(g, k, [rel_slow[:, j:j + 1] for j in range(TILES)], sel_ready)
                dve.wait_ge(win_done, g + 1)
                dve.wait_ge(slow_added, (g + 1) * (NWIN - 1) + 1)
                add_window(win_sum[k % 2], NP - WIN, agg_added)

            def step(s, k, fits, q):
                edge = isinstance(s, int)
                mid = not edge or 0 <= s - 1 < NG
                end = not edge or 0 <= s - 2 < NG
                if end and fits:
                    start = dve.value_load(base_i[0:1, bass.ds(s - 2, 1)], min_val=0, max_val=N)
                if mid:
                    clamp2(s - 1, k - 1)
                    if fits:
                        select_own(s - 1, (k - 1) % UNROLL)
                if not edge or s + 1 < NG:
                    clamp1(s + 1, k + 1)
                if mid:
                    filt(s - 1, k - 1)
                if end and fits:
                    add_own(s - 2, win_sum[k % 2], start)
                if not edge or s + 1 < NG:
                    act1(s + 1, k + 1)
                if mid:
                    message(s - 1, (k - 1) % UNROLL, q + (k - 1) // UNROLL)
                if end and not fits:
                    add_all(s - 2, (k - 2) % UNROLL)

            def last_messages(fits):
                g, k = NG - 1, (NG - 1) % UNROLL
                start = [dve.value_load(base_i[0:1, n:n + 1], min_val=0, max_val=N) for n in (g - 1, g)] if fits else []
                if fits:
                    select_own(g, k)
                for half in range(2):
                    clamp2(g, k, half)
                for half in range(2):
                    filt(g, k, half)
                    message(g, k, g // UNROLL, half)
                for n in (g - 1, g):
                    if fits:
                        add_own(n, win_sum[n % 2] if n < g else last_sum, start[n - g + 1])
                    else:
                        add_all(n, n % UNROLL)

            dve.wait_ge(cut_ready, 1)
            dve.wait_ge(windows_ready, 1)
            dve.wait_ge(slow_added, 1)
            widest_span = dve.value_load(widest_i[0:1, 0:1], min_val=0, max_val=NP)

            def edges(fits):
                for s in range(UNROLL):
                    step(s, s, fits, 0)
                with dve.Fori(1, NG // UNROLL - 1) as q:
                    for k in range(UNROLL):
                        step(q * UNROLL + k, k, fits, q)
                for s in range(NG - UNROLL, NG):
                    step(s, s % UNROLL, fits, s // UNROLL)
                last_messages(fits)

            with dve.If(widest_span < WIN):
                edges(True)
            with dve.Else():
                edges(False)

            steps = [0]

            def then(ins):
                steps[0] += 1
                ins.then_inc(out_step, 1)
                dve.wait_ge(out_step, steps[0])

            def o_clamp(c):
                n = chunk_tiles(c) * P
                dve.wait_ge(oexp_done, c + 1)
                ev = e1[:, c % 2, :].rearrange("p (h n) -> p h n", h=KF)[:, :, 0:n]
                nc.vector.tensor_scalar(ev, ev, EXP_MAX, None, ALU.min).then_inc(oclamp_done, 1)

            def o_act(c):
                n = chunk_tiles(c) * P
                dve.wait_ge(oln_done, c + 1)
                if c >= 2:
                    dve.wait_ge(o2_done, c - 1)
                for h in range(KF):
                    last = nc.vector.scalar_tensor_tensor(
                        out=a1[:, c % 2, h * GE:h * GE + n], in0=u1[c % 2][:, h, 0:n], scalar=o1_bias_ln2[:, h:h + 1],
                        in1=e1[:, c % 2, h * GE:h * GE + n], op0=ALU.add, op1=ALU.max)
                last.then_inc(t_ready, 1)

            def o_sum(c):
                n = chunk_tiles(c)
                ts = slice(first_tile(c), first_tile(c) + n)
                dve.wait_ge(o2_done, c + 1)
                nc.vector.tensor_tensor(z[:, ts, :].rearrange("p t f -> p (t f)"),
                                        u2[c % 2].rearrange("p a f -> p (a f)")[:, 0:n * F],
                                        z[:, ts, :].rearrange("p t f -> p (t f)"), ALU.add).then_inc(z_ready, 1)
                dve.wait_ge(z_ready, c + 1)
                for t in range(first_tile(c), first_tile(c) + n):
                    last = nc.vector.bn_stats(stats[:, t, :], z[:, t, :])
                then(last)
                for t in range(first_tile(c), first_tile(c) + n):
                    last = nc.vector.bn_aggr(mv[:, t, :], stats[:, t, :])
                then(last)
                nc.vector.tensor_scalar(var_eps[:, ts], mv[:, ts, 1], EPS, None, ALU.add).then_inc(var_ready, 1)

            def o_scale(c):
                ts = slice(first_tile(c), first_tile(c) + chunk_tiles(c))
                dve.wait_ge(rstd0_ready, c + 1)
                then(nc.vector.tensor_tensor(newton[:, ts], rstd0[:, ts], rstd0[:, ts], ALU.mult))
                then(nc.vector.scalar_tensor_tensor(out=newton[:, ts], in0=newton[:, ts], scalar=-0.5,
                                                    in1=var_eps[:, ts], op0=ALU.mult, op1=ALU.mult))
                then(nc.vector.scalar_tensor_tensor(out=rstd[:, ts], in0=newton[:, ts], scalar=1.5,
                                                    in1=rstd0[:, ts], op0=ALU.add, op1=ALU.mult))
                nc.vector.scalar_tensor_tensor(out=shift[:, ts], in0=mv[:, ts, 0], scalar=-1.0,
                                               in1=rstd[:, ts], op0=ALU.mult, op1=ALU.mult).then_inc(scale_ready, 1)

            for c in range(CHUNKS + 2):
                if c < CHUNKS:
                    o_clamp(c)
                if c >= 2:
                    o_scale(c - 2)
                if c < CHUNKS:
                    o_act(c)
                if c == 1:
                    dve.wait_ge(xb_ready, 1)
                if 1 <= c <= CHUNKS:
                    o_sum(c - 1)


_WEIGHTS = ['aw_W', 'aw_b', 'm1_W', 'm1_b', 'm2_W', 'm2_b', 'o1_W', 'o1_b', 'o2_W', 'o2_b']


def kernel(**inputs):
    import numpy as np
    import concourse.bacc as bacc
    from concourse import mybir as mb
    from concourse.bass_utils import run_bass_kernel_spmd

    x = np.asarray(inputs["x"])
    n, f = x.shape
    edges = inputs["src"].shape[0]
    attrs = inputs["edge_attr_50"].shape[1]
    nodes_pad = -(-n // P) * P
    edges_pad = -(-edges // (GE * UNROLL)) * GE * UNROLL
    rows = P // 2
    more = edges_pad - edges

    def by_tile(a, fill):
        a = np.pad(np.asarray(a), (0, more), constant_values=fill)
        return np.ascontiguousarray(a.reshape(-1, P).T)

    x_pad = np.pad(x, ((0, nodes_pad - n), (0, 0)))
    attr = np.zeros((rows, edges_pad), x.dtype)
    attr[:attrs, :edges] = np.asarray(inputs["edge_attr_50"]).T
    attr[attrs] = 1
    arrays = {
        "x": x_pad,
        "xT": np.ascontiguousarray(x_pad.T),
        "attrT": attr,
        "src": by_tile(inputs["src"], 0),
        "dst": by_tile(inputs["dst"], n),
        "dst_groups": np.pad(np.asarray(inputs["dst"]), (0, more), constant_values=n).reshape(-1, GE),
        "edge_weight": by_tile(inputs["edge_weight"], 0),
    }
    for w in _WEIGHTS:
        arrays[w] = np.ascontiguousarray(inputs["L0_gnn_" + w])
    arrays["o1_b"] = np.ascontiguousarray(arrays["o1_b"].reshape(-1, P).T)

    nc = bacc.Bacc("TRN2", target_bir_lowering=False, num_devices=1)
    args = {k: nc.dram_tensor(f"in_{k}", a.shape, mb.dt.from_np(a.dtype), kind="ExternalInput").ap()
            for k, a in arrays.items()}
    out = nc.dram_tensor("out_0", (n, f), mb.dt.float32, kind="ExternalOutput").ap()
    gnn_resnorm_kernel(nc, **args, out=out)
    r = run_bass_kernel_spmd(nc, [{f"in_{k}": a for k, a in arrays.items()}], core_ids=[0])
    return r.results[0]["out_0"]
```
